# Optimizing a Trainium2 kernel written in Bass

```python
import numpy as np
import jax
import jax.numpy as jnp

def _softmax(x, axis=-1):
    return jax.nn.softmax(x, axis=axis)

def _gelu(x):
    return jax.nn.gelu(x, approximate=True)

def _silu(x):
    return jax.nn.silu(x)

def _sigmoid(x):
    return jax.nn.sigmoid(x)

def _layernorm(x, axis=-1, eps=1e-05):
    m = jnp.mean(x, axis=axis, keepdims=True)
    v = jnp.var(x, axis=axis, keepdims=True)
    return (x - m) / jnp.sqrt(v + eps)

def _scatter_add(tgt, idx, src, axis=0):
    return tgt.at[idx].add(src)

def _segment_sum(src, seg, n):
    return jax.ops.segment_sum(src, seg, n)
kernel_name = 'mk_decoder_postln_d1_seqx_r8_03886c'

def setup_inputs(seed: int=0):
    np.random.seed(seed)
    _w = jnp.asarray

    def _rec_inputs():
        import jax
        import jax.numpy as jnp
        _rk = jax.random.key(seed)
        x = 0.000341 + 1 * jax.random.normal(jax.random.fold_in(_rk, 1), (4, 512, 128), jnp.float32)
        _lenS = 512 - jax.random.randint(jax.random.fold_in(_rk, 7), (4,), 0, max(1, 512 // 4) + 1, jnp.int32)
        _lenS2 = 32 - jax.random.randint(jax.random.fold_in(_rk, 8), (4,), 0, max(1, 32 // 4) + 1, jnp.int32)
        _ctx_1024P = jax.random.normal(jax.random.fold_in(_rk, 11), (4, 16, 128), jnp.float32)
        _ctx_1024c = jax.random.dirichlet(jax.random.fold_in(_rk, 511), 0.3 * jnp.ones((16,), jnp.float32), (4, 32))
        _ctx_1024t = jnp.einsum('bsk,bkd->bsd', _ctx_1024c, _ctx_1024P)
        _ctx_1024t = _ctx_1024t * jax.lax.rsqrt(jnp.mean(jnp.square(_ctx_1024t)) + 1e-12) * 0.953939
        ctx_1024 = -0.000392918 + 0.999932 * (_ctx_1024t + 0.3 * jax.random.normal(jax.random.fold_in(_rk, 611), (4, 32, 128), jnp.float32))
        _validS = jnp.arange(512)[None, :] < _lenS[:, None]
        _validS2 = jnp.arange(32)[None, :] < _lenS2[:, None]
        _causal = jnp.tril(jnp.ones((512, 512), dtype=bool))
        mask_1_bf0 = jnp.logical_not(jnp.ones((1,), dtype=bool))
        return (x, ctx_1024, mask_1_bf0)
    x, ctx_1024, mask_1_bf0 = _rec_inputs()

    def _L0_attn_setup():
        import jax, jax.numpy as jnp
        import numpy as np
        B, S, D_MODEL = (2, 256, 128)
        H, D = (16, 64)
        D_INNER = H * D
        EPS = 1e-05
        key = jax.random.key(seed)
        ks = jax.random.split(key, 10)
        sc = 0.02
        return {'x': jax.random.normal(ks[0], (B, S, D_MODEL), dtype=jnp.float32), 'Wq': jax.random.normal(ks[1], (D_MODEL, D_INNER), dtype=jnp.float32) * sc, 'Wk': jax.random.normal(ks[2], (D_MODEL, D_INNER), dtype=jnp.float32) * sc, 'Wv': jax.random.normal(ks[3], (D_MODEL, D_INNER), dtype=jnp.float32) * sc, 'Wg': jax.random.normal(ks[4], (D_MODEL, D_INNER), dtype=jnp.float32) * sc, 'Wa': jax.random.normal(ks[5], (D_MODEL, H), dtype=jnp.float32) * sc, 'ba': jax.random.normal(ks[6], (H,), dtype=jnp.float32) * sc, 'Wo': jax.random.normal(ks[7], (D_INNER, D_MODEL), dtype=jnp.float32) * sc, 'gn_w': jnp.ones((D_INNER,), dtype=jnp.float32), 'gn_b': jnp.zeros((D_INNER,), dtype=jnp.float32)}
    _L0_attn_all = _L0_attn_setup()
    _L0_attn_in = {k: v for k, v in _L0_attn_all.items() if k in ('Wq', 'Wk', 'Wv', 'Wg', 'Wa', 'ba', 'Wo', 'gn_w', 'gn_b')}
    del _L0_attn_all

    def _L0_xattn_setup():
        import jax, jax.numpy as jnp
        import numpy as np
        B, SQ, SK, D_IN, D_H, D_OUT = (8, 256, 256, 128, 128, 128)
        key0 = jax.random.key(seed)
        ks = jax.random.split(key0, 8)
        return {'key': jax.random.normal(ks[0], (B, SK, D_IN), jnp.float32), 'value': jax.random.normal(ks[1], (B, SK, D_H), jnp.float32), 'query': jax.random.normal(ks[2], (B, SQ, D_IN), jnp.float32), 'mask': jnp.zeros((1,), jnp.bool_), 'inv_scale_factor': 32, 'W1': jax.random.normal(ks[3], (D_H, D_IN), jnp.float32) * (1.0 / np.sqrt(D_IN)), 'b1': jax.random.normal(ks[4], (D_H,), jnp.float32) * 0.01, 'W2': jax.random.normal(ks[5], (D_H, D_IN), jnp.float32) * (1.0 / np.sqrt(D_IN)), 'b2': jax.random.normal(ks[6], (D_H,), jnp.float32) * 0.01, 'W3': jax.random.normal(ks[7], (D_OUT, D_H), jnp.float32) * (1.0 / np.sqrt(D_H))}
    _L0_xattn_all = _L0_xattn_setup()
    _L0_xattn_in = {k: v for k, v in _L0_xattn_all.items() if k in ('W1', 'b1', 'W2', 'b2', 'W3')}
    del _L0_xattn_all

    def _L0_ffn_setup():
        import jax, jax.numpy as jnp
        import numpy as np
        DIM = 128
        DEPTH = 6
        HEADS = 16
        DIM_HEAD = 64
        WINDOW = 32
        INNER = HEADS * DIM_HEAD
        DIM_INNER = int(DIM * 4 * 2 / 3)
        QK_SCALE = 8.0

        def shift_tokens(t):
            a, s = jnp.split(t, 2, -1)
            s = jnp.pad(s, ((0, 0), (1, 0), (0, 0)))[:, :-1]
            return jnp.concatenate([a, s], -1)

        def l2norm(t):
            return t / jnp.maximum(jnp.linalg.norm(t, axis=-1, keepdims=True), 1e-12)

        def rotate_half(x):
            x1, x2 = jnp.split(x, 2, -1)
            return jnp.concatenate([-x2, x1], -1)

        def rotary_tables(n):
            half = jnp.arange(0, DIM_HEAD, 2, dtype=jnp.float32)
            inv_freq = 1.0 / 10000.0 ** (half / DIM_HEAD)
            t = jnp.arange(n, dtype=jnp.float32)
            freqs = t[:, None] * inv_freq[None, :]
            freqs = jnp.concatenate([freqs, freqs], -1)
            base_scale = (half + 0.4 * DIM_HEAD) / (1.4 * DIM_HEAD)
            power = (t - n // 2) / (WINDOW // 2)
            scale = base_scale[None, :] ** power[:, None]
            scale = jnp.concatenate([scale, scale], -1)
            return (freqs, scale)

        def local_attention(q, k, v):
            b, h, n, d = q.shape
            w = WINDOW
            nw = n // w
            bq = q.reshape(b, h, nw, w, d)
            bk = k.reshape(b, h, nw, w, d)
            bv = v.reshape(b, h, nw, w, d)

            def look(t):
                p = jnp.pad(t, ((0, 0), (0, 0), (1, 0), (0, 0), (0, 0)))
                return jnp.concatenate([p[:, :, :nw], p[:, :, 1:]], axis=3)
            bk2, bv2 = (look(bk), look(bv))
            seq = jnp.arange(n).reshape(nw, w)
            seq_p = jnp.pad(seq, ((1, 0), (0, 0)), constant_values=-1)
            jt = jnp.concatenate([seq_p[:nw], seq_p[1:]], axis=1)
            it = seq[:, :, None]
            jb = jt[:, None, :]
            mask = (it < jb) | (it > jb + w) | (jb == -1)
            sim = jnp.einsum('bhwie,bhwje->bhwij', bq, bk2) * QK_SCALE
            sim = jnp.where(mask, -jnp.finfo(sim.dtype).max, sim)
            attn = jax.nn.softmax(sim, -1)
            out = jnp.einsum('bhwij,bhwje->bhwie', attn, bv2)
            return out.reshape(b, h, n, d)

        def attn_layer(x, Wqkv, qs, ksc, Wo):
            b, n, _ = x.shape
            qkv = x @ Wqkv
            q, k, v = jnp.split(qkv, 3, -1)
            sh = lambda t: t.reshape(b, n, HEADS, DIM_HEAD).transpose(0, 2, 1, 3)
            q, k, v = (sh(q), sh(k), sh(v))
            q = l2norm(q) * qs
            k = l2norm(k) * ksc
            freqs, scale = rotary_tables(n)
            cos, sin = (jnp.cos(freqs), jnp.sin(freqs))
            q = q * cos * scale + rotate_half(q) * sin * scale
            inv = 1.0 / scale
            k = k * cos * inv + rotate_half(k) * sin * inv
            out = local_attention(q, k, v)
            out = out.transpose(0, 2, 1, 3).reshape(b, n, INNER)
            return out @ Wo

        def ffn_layer(x, g, bln, W1, b1, W2, b2):
            mu = x.mean(-1, keepdims=True)
            var = ((x - mu) ** 2).mean(-1, keepdims=True)
            xn = (x - mu) / jnp.sqrt(var + 1e-05) * g + bln
            hg = xn @ W1 + b1
            a, gate = jnp.split(hg, 2, -1)
            return a * jax.nn.gelu(gate, approximate=False) @ W2 + b2
        key = jax.random.key(seed)
        ks = jax.random.split(key, 8)
        B, N = (2, 256)
        init = lambda k, shape: jax.random.normal(k, shape, jnp.float32) * 0.02
        return {'x': jax.random.normal(ks[0], (B, N, DIM), jnp.float32), 'Wqkv': init(ks[1], (DEPTH, DIM, 3 * INNER)), 'q_scale': jnp.ones((DEPTH, DIM_HEAD), jnp.float32), 'k_scale': jnp.ones((DEPTH, DIM_HEAD), jnp.float32), 'Wo': init(ks[2], (DEPTH, INNER, DIM)), 'ln_g': jnp.ones((DEPTH, DIM), jnp.float32), 'ln_b': jnp.zeros((DEPTH, DIM), jnp.float32), 'W1': init(ks[3], (DEPTH, DIM, 2 * DIM_INNER)), 'b1': jnp.zeros((DEPTH, 2 * DIM_INNER), jnp.float32), 'W2': init(ks[4], (DEPTH, DIM_INNER, DIM)), 'b2': jnp.zeros((DEPTH, DIM), jnp.float32)}
    _L0_ffn_all = _L0_ffn_setup()
    _L0_ffn_in = {k: v for k, v in _L0_ffn_all.items() if k in ('Wqkv', 'q_scale', 'k_scale', 'Wo', 'ln_g', 'ln_b', 'W1', 'b1', 'W2', 'b2')}
    del _L0_ffn_all
    return {'x': x, 'ctx_1024': ctx_1024, 'mask_1_bf0': mask_1_bf0, 'L0_attn_Wq': _L0_attn_in['Wq'], 'L0_attn_Wk': _L0_attn_in['Wk'], 'L0_attn_Wv': _L0_attn_in['Wv'], 'L0_attn_Wg': _L0_attn_in['Wg'], 'L0_attn_Wa': _L0_attn_in['Wa'], 'L0_attn_ba': _L0_attn_in['ba'], 'L0_attn_Wo': _L0_attn_in['Wo'], 'L0_attn_gn_w': _L0_attn_in['gn_w'], 'L0_attn_gn_b': _L0_attn_in['gn_b'], 'L0_xattn_W1': _L0_xattn_in['W1'], 'L0_xattn_b1': _L0_xattn_in['b1'], 'L0_xattn_W2': _L0_xattn_in['W2'], 'L0_xattn_b2': _L0_xattn_in['b2'], 'L0_xattn_W3': _L0_xattn_in['W3'], 'L0_ffn_Wqkv': _L0_ffn_in['Wqkv'], 'L0_ffn_q_scale': _L0_ffn_in['q_scale'], 'L0_ffn_k_scale': _L0_ffn_in['k_scale'], 'L0_ffn_Wo': _L0_ffn_in['Wo'], 'L0_ffn_ln_g': _L0_ffn_in['ln_g'], 'L0_ffn_ln_b': _L0_ffn_in['ln_b'], 'L0_ffn_W1': _L0_ffn_in['W1'], 'L0_ffn_b1': _L0_ffn_in['b1'], 'L0_ffn_W2': _L0_ffn_in['W2'], 'L0_ffn_b2': _L0_ffn_in['b2']}

def reference(x, ctx_1024, mask_1_bf0, L0_attn_Wq, L0_attn_Wk, L0_attn_Wv, L0_attn_Wg, L0_attn_Wa, L0_attn_ba, L0_attn_Wo, L0_attn_gn_w, L0_attn_gn_b, L0_xattn_W1, L0_xattn_b1, L0_xattn_W2, L0_xattn_b2, L0_xattn_W3, L0_ffn_Wqkv, L0_ffn_q_scale, L0_ffn_k_scale, L0_ffn_Wo, L0_ffn_ln_g, L0_ffn_ln_b, L0_ffn_W1, L0_ffn_b1, L0_ffn_W2, L0_ffn_b2):
    import jax
    import jax.numpy as jnp

    def _L0_attn_ref(x, Wq, Wk, Wv, Wg, Wa, ba, Wo, gn_w, gn_b):
        import jax, jax.numpy as jnp
        import numpy as np
        B, S, D_MODEL = (2, 256, 128)
        H, D = (16, 64)
        D_INNER = H * D
        EPS = 1e-05
        b, s, _ = x.shape
        q = jax.nn.silu(jnp.einsum('bsm,md->bsd', x, Wq).reshape(b, s, H, D).transpose(0, 2, 1, 3))
        k = jax.nn.silu(jnp.einsum('bsm,md->bsd', x, Wk).reshape(b, s, H, D).transpose(0, 2, 1, 3))
        v = jnp.einsum('bsm,md->bsd', x, Wv).reshape(b, s, H, D).transpose(0, 2, 1, 3)
        log_alpha = -jax.nn.softplus(jnp.einsum('bsm,mh->bsh', x, Wa) + ba)
        cum = jnp.cumsum(log_alpha, axis=1).transpose(0, 2, 1)
        diff = cum[:, :, :, None] - cum[:, :, None, :]
        causal = jnp.tril(jnp.ones((s, s), dtype=bool))
        decay = jnp.exp(jnp.where(causal, diff, -jnp.inf))
        attn = jnp.einsum('bhid,bhjd->bhij', q, k) * decay
        o = jnp.einsum('bhij,bhjd->bhid', attn, v)
        o = o.transpose(0, 2, 1, 3)
        mean = jnp.mean(o, axis=(1, 3), keepdims=True)
        var = jnp.var(o, axis=(1, 3), keepdims=True)
        o = (o - mean) / jnp.sqrt(var + EPS)
        o = o * gn_w.reshape(H, D) + gn_b.reshape(H, D)
        o = o.reshape(b, s, H * D)
        gate = jax.nn.sigmoid(jnp.einsum('bsm,md->bsd', x, Wg))
        return jnp.einsum('bsd,dm->bsm', o * gate, Wo)

    def _L0_xattn_ref(key, value, query, mask, inv_scale_factor, W1, b1, W2, b2, W3):
        import jax, jax.numpy as jnp
        import numpy as np
        B, SQ, SK, D_IN, D_H, D_OUT = (8, 256, 256, 128, 128, 128)
        q = jnp.einsum('bqd,hd->bqh', query, W1) + b1
        k = jnp.einsum('bkd,hd->bkh', key, W2) + b2
        qk = jnp.einsum('bqh,bkh->bqk', q, k) / inv_scale_factor
        attn = jax.nn.softmax(qk, axis=-1)
        ctx = jnp.einsum('bqk,bkh->bqh', attn, value)
        out = jnp.einsum('bqh,oh->bqo', ctx, W3)
        return out

    def _L0_ffn_ref(x, Wqkv, q_scale, k_scale, Wo, ln_g, ln_b, W1, b1, W2, b2):
        import jax, jax.numpy as jnp
        import numpy as np
        DIM = 128
        DEPTH = 6
        HEADS = 16
        DIM_HEAD = 64
        WINDOW = 32
        INNER = HEADS * DIM_HEAD
        DIM_INNER = int(DIM * 4 * 2 / 3)
        QK_SCALE = 8.0

        def shift_tokens(t):
            a, s = jnp.split(t, 2, -1)
            s = jnp.pad(s, ((0, 0), (1, 0), (0, 0)))[:, :-1]
            return jnp.concatenate([a, s], -1)

        def l2norm(t):
            return t / jnp.maximum(jnp.linalg.norm(t, axis=-1, keepdims=True), 1e-12)

        def rotate_half(x):
            x1, x2 = jnp.split(x, 2, -1)
            return jnp.concatenate([-x2, x1], -1)

        def rotary_tables(n):
            half = jnp.arange(0, DIM_HEAD, 2, dtype=jnp.float32)
            inv_freq = 1.0 / 10000.0 ** (half / DIM_HEAD)
            t = jnp.arange(n, dtype=jnp.float32)
            freqs = t[:, None] * inv_freq[None, :]
            freqs = jnp.concatenate([freqs, freqs], -1)
            base_scale = (half + 0.4 * DIM_HEAD) / (1.4 * DIM_HEAD)
            power = (t - n // 2) / (WINDOW // 2)
            scale = base_scale[None, :] ** power[:, None]
            scale = jnp.concatenate([scale, scale], -1)
            return (freqs, scale)

        def local_attention(q, k, v):
            b, h, n, d = q.shape
            w = WINDOW
            nw = n // w
            bq = q.reshape(b, h, nw, w, d)
            bk = k.reshape(b, h, nw, w, d)
            bv = v.reshape(b, h, nw, w, d)

            def look(t):
                p = jnp.pad(t, ((0, 0), (0, 0), (1, 0), (0, 0), (0, 0)))
                return jnp.concatenate([p[:, :, :nw], p[:, :, 1:]], axis=3)
            bk2, bv2 = (look(bk), look(bv))
            seq = jnp.arange(n).reshape(nw, w)
            seq_p = jnp.pad(seq, ((1, 0), (0, 0)), constant_values=-1)
            jt = jnp.concatenate([seq_p[:nw], seq_p[1:]], axis=1)
            it = seq[:, :, None]
            jb = jt[:, None, :]
            mask = (it < jb) | (it > jb + w) | (jb == -1)
            sim = jnp.einsum('bhwie,bhwje->bhwij', bq, bk2) * QK_SCALE
            sim = jnp.where(mask, -jnp.finfo(sim.dtype).max, sim)
            attn = jax.nn.softmax(sim, -1)
            out = jnp.einsum('bhwij,bhwje->bhwie', attn, bv2)
            return out.reshape(b, h, n, d)

        def attn_layer(x, Wqkv, qs, ksc, Wo):
            b, n, _ = x.shape
            qkv = x @ Wqkv
            q, k, v = jnp.split(qkv, 3, -1)
            sh = lambda t: t.reshape(b, n, HEADS, DIM_HEAD).transpose(0, 2, 1, 3)
            q, k, v = (sh(q), sh(k), sh(v))
            q = l2norm(q) * qs
            k = l2norm(k) * ksc
            freqs, scale = rotary_tables(n)
            cos, sin = (jnp.cos(freqs), jnp.sin(freqs))
            q = q * cos * scale + rotate_half(q) * sin * scale
            inv = 1.0 / scale
            k = k * cos * inv + rotate_half(k) * sin * inv
            out = local_attention(q, k, v)
            out = out.transpose(0, 2, 1, 3).reshape(b, n, INNER)
            return out @ Wo

        def ffn_layer(x, g, bln, W1, b1, W2, b2):
            mu = x.mean(-1, keepdims=True)
            var = ((x - mu) ** 2).mean(-1, keepdims=True)
            xn = (x - mu) / jnp.sqrt(var + 1e-05) * g + bln
            hg = xn @ W1 + b1
            a, gate = jnp.split(hg, 2, -1)
            return a * jax.nn.gelu(gate, approximate=False) @ W2 + b2
        for i in range(DEPTH):
            x = attn_layer(shift_tokens(x), Wqkv[i], q_scale[i], k_scale[i], Wo[i]) + x
            x = ffn_layer(shift_tokens(x), ln_g[i], ln_b[i], W1[i], b1[i], W2[i], b2[i]) + x
        return x
    x = _layernorm(x + _L0_attn_ref(x, L0_attn_Wq, L0_attn_Wk, L0_attn_Wv, L0_attn_Wg, L0_attn_Wa, L0_attn_ba, L0_attn_Wo, L0_attn_gn_w, L0_attn_gn_b), axis=-1)
    x = _layernorm(x + _L0_xattn_ref(ctx_1024, ctx_1024, x, mask_1_bf0, 32, L0_xattn_W1, L0_xattn_b1, L0_xattn_W2, L0_xattn_b2, L0_xattn_W3), axis=-1)
    x = _layernorm(x + _L0_ffn_ref(x, L0_ffn_Wqkv, L0_ffn_q_scale, L0_ffn_k_scale, L0_ffn_Wo, L0_ffn_ln_g, L0_ffn_ln_b, L0_ffn_W1, L0_ffn_b1, L0_ffn_W2, L0_ffn_b2), axis=-1)
    return x

_drawn_inputs = setup_inputs


def setup_inputs(seed=0):
    import zlib

    import numpy as np

    out = dict(_drawn_inputs(seed))
    spreads = {'L0_attn_gn_w': (1.0, 0.2),
     'L0_attn_gn_b': (0.0, 0.31),
     'L0_ffn_q_scale': (1.0, 0.6),
     'L0_ffn_k_scale': (1.0, 0.6),
     'L0_ffn_ln_g': (1.0, 0.6),
     'L0_ffn_ln_b': (0.0, 0.8),
     'L0_ffn_b1': (0.0, 0.8),
     'L0_ffn_b2': (0.0, 0.1)}
    factors = {'L0_attn_Wa': 3.121,
     'L0_attn_ba': 29.971,
     'L0_xattn_b1': 49.54,
     'L0_xattn_b2': 64.0,
     'L0_ffn_W1': 3.684,
     'L0_ffn_W2': 3.617}
    for name, (base, spread) in spreads.items():
        noise = np.random.default_rng([zlib.crc32(name.encode()), seed]).standard_normal(out[name].shape)
        drawn = base * np.exp(spread * noise) if base else spread * noise
        out[name] = jnp.asarray(drawn.astype(out[name].dtype))
    for name, factor in factors.items():
        out[name] = (out[name] * factor).astype(out[name].dtype)
    return out
```

```python
import numpy as np
import concourse.bass as bass
from concourse import mybir
F32 = mybir.dt.float32
ALU = mybir.AluOpType
ACT = mybir.ActivationFunctionType
AX = mybir.AxisListType.X
PARTS = 128

def due(value):
    return not isinstance(value, int) or value > 0

def carver(arena):
    at = [0]

    def carve(*shape):
        n = int(np.prod(shape))
        a = at[0]
        at[0] += n
        v = arena[:, a:a + n]
        if len(shape) == 2:
            v = v.rearrange('p (a b) -> p a b', b=shape[1])
        if len(shape) == 3:
            v = v.rearrange('p (a b c) -> p a b c', b=shape[1], c=shape[2])
        return v
    return carve

def decoder(nc, io, LAYERS=6):
    BATCHES = 4
    SEQ = 512
    BLOCKS = 4
    FFN_PASSES = LAYERS * BATCHES
    ALL_BLOCKS = FFN_PASSES * BLOCKS

    def sb(name, shape):
        return nc.alloc_sbuf_tensor(name, shape, F32)
    x_all = sb('X', [PARTS, BATCHES * SEQ])
    x_shift = sb('XS', [PARTS, 32 + SEQ])
    w_q = sb('WQ', [PARTS, 1024])
    w_k = sb('WK', [PARTS, 1024])
    w_v = sb('WV', [PARTS, 1024])
    w_o = sb('WO', [PARTS, 8, PARTS])
    w_1 = sb('W1', [PARTS, 682])
    w_2 = sb('W2', [PARTS, 3, PARTS])
    layer_vecs = sb('vec', [PARTS, 9 * LAYERS])
    rotary_base = sb('base', [PARTS, 4, 4, 64])
    rotary_tab = sb('tab', [PARTS, 4, 4, 64])
    qk_scales = sb('scl', [PARTS, 4, LAYERS, 64])
    ident = sb('ident', [PARTS, PARTS])
    mean_w = sb('mean_w', [PARTS, PARTS])
    window_mask = sb('mask', [PARTS, 2, 64])
    tiny = sb('tiny', [PARTS, 2])
    arena = sb('work', [PARTS, 30900])
    cv = carver(arena)
    squares = cv(2, 1024)
    cos_part = cv(2, 1024)
    sin_part = cv(2, 1024)
    qk_norm = cv(2, 1024)
    sq_sums = sb('SS', [PARTS, 2, 16])
    sq_clamped = sb('SL', [PARTS, 32])
    norm_logs = sb('LS', [PARTS, 32])
    inv_norms = sb('RS', [PARTS, 2, 16])
    q_t = cv(8, 128)
    k_t = sb('KT', [PARTS, 8, 32 + 256])
    v_win = cv(2, 4, 512)
    heads = cv(1024)
    scores_sb = cv(8, 2, 64)
    row_max = sb('MX', [PARTS, 16])
    probs = cv(8, 2, 64)
    row_sum = sb('LE', [PARTS, 16])
    row_inv = sb('RL', [PARTS, 16])
    probs_t = cv(8, 128)
    heads_t = cv(8, SEQ)
    ffn_x = sb('YS', [PARTS, SEQ])
    centred = sb('YC', [PARTS, SEQ])
    spread = sb('YQ', [PARTS, SEQ])
    normed = sb('YR', [PARTS, SEQ])
    ffn_in = sb('YN', [PARTS, SEQ])
    gate = cv(3, SEQ)
    hidden = cv(3, SEQ)
    assert BATCHES * BLOCKS == 16
    BF16 = mybir.dt.bfloat16
    av = carver(arena)
    q_act = av(8, SEQ)
    k_act = av(8, SEQ)
    gate_act = av(8, SEQ)
    attn_heads = av(8, SEQ)
    v_chunk = av(1024)
    seg_operand = av(16, 128)
    pair_decay = av(16, 128)
    pair_scores = av(16, 128)
    head_decay = av(8, 128)
    q_decayed = av(8, 128)
    k_decayed = av(1024)
    state = av(8, 64)
    w_gate = av(1024)
    x_batch = ffn_in
    Z = av(64)
    alpha_tmp = av(64)
    alpha_soft = av(64)
    log_alpha = av(64)
    tail_decay = av(4, 16)
    triangles = av(2, 128)
    head_mean_w = av(128)
    chan_stats = av(8, 6)
    chan_mean_var = av(8, 2)
    group_vars = av(2, 8)
    group_tmp = av(64)
    norm_affine = av(3, 8)
    w_alpha = av(16)
    b_alpha = av(16)
    ones = av(128)
    x_residual = sb('X0', [PARTS, BATCHES * SEQ])
    ctx_t = av(128)
    w_cross = av(3, 128)
    b_cross = av(2)
    ctx_k = av(128)
    ctx_k_folded = av(128)
    ctx_k_bias = av(128)
    ctx_v = av(4, 128)
    ctx_v_batch = av(128)
    cross_p = av(4, 32)
    cross_stat = av(4)
    cross_p_t = pair_decay.rearrange('p a b -> p (a b)')[:, 0:SEQ]
    ident_bf16 = nc.alloc_sbuf_tensor('ident_bf16', [PARTS, 128], BF16)
    causal_bf16_mask = nc.alloc_sbuf_tensor('mkb', [PARTS, 128], BF16)
    psum = nc.alloc_psum_tensor('ps', [PARTS, 8, 512], F32)
    q_psum = psum[:, 0:2, :]
    k_psum = psum[:, 2:4, :]
    psum_a = psum[:, 4:6, :]
    psum_b = psum[:, 6:8, :]
    flat = lambda ap: ap.rearrange('p a b -> p (a b)')
    x_loaded = nc.alloc_semaphore('x_loaded')
    wq_loaded = nc.alloc_semaphore('wq_loaded')
    wk_loaded = nc.alloc_semaphore('wk_loaded')
    wv_loaded = nc.alloc_semaphore('wv_loaded')
    wo_loaded = nc.alloc_semaphore('wo_loaded')
    w1_loaded = nc.alloc_semaphore('w1_loaded')
    w2_loaded = nc.alloc_semaphore('w2_loaded')
    constants_loaded = nc.alloc_semaphore('constants_loaded')
    zeroed = nc.alloc_semaphore('zeroed')
    block_shifted = nc.alloc_semaphore('block_shifted')
    q_projected = nc.alloc_semaphore('q_projected')
    k_projected = nc.alloc_semaphore('k_projected')
    q_squared = nc.alloc_semaphore('q_squared')
    k_squared = nc.alloc_semaphore('k_squared')
    q_sums = nc.alloc_semaphore('q_sums')
    k_sums = nc.alloc_semaphore('k_sums')
    sums_clamped = nc.alloc_semaphore('sums_clamped')
    norms_log = nc.alloc_semaphore('norms_log')
    inverse_norms = nc.alloc_semaphore('inverse_norms')
    tables_scaled = nc.alloc_semaphore('tables_scaled')
    q_cos = nc.alloc_semaphore('q_cos')
    q_sin = nc.alloc_semaphore('q_sin')
    k_cos = nc.alloc_semaphore('k_cos')
    k_sin = nc.alloc_semaphore('k_sin')
    q_rotated = nc.alloc_semaphore('q_rotated')
    k_rotated = nc.alloc_semaphore('k_rotated')
    q_normed = nc.alloc_semaphore('q_normed')
    k_normed = nc.alloc_semaphore('k_normed')
    q_turned = nc.alloc_semaphore('q_turned')
    k_turned = nc.alloc_semaphore('k_turned')
    q_turned_copied = nc.alloc_semaphore('q_turned_copied')
    k_turned_copied = nc.alloc_semaphore('k_turned_copied')
    values_01 = nc.alloc_semaphore('values_01')
    values_23 = nc.alloc_semaphore('values_23')
    values_01_copied = nc.alloc_semaphore('values_01_copied')
    values_23_copied = nc.alloc_semaphore('values_23_copied')
    scores_ready = nc.alloc_semaphore('scores_ready')
    scores_masked = nc.alloc_semaphore('scores_masked')
    scores_max = nc.alloc_semaphore('scores_max')
    scores_shifted = nc.alloc_semaphore('scores_shifted')
    probs_exp = nc.alloc_semaphore('probs_exp')
    probs_sum = nc.alloc_semaphore('probs_sum')
    probs_inverse = nc.alloc_semaphore('probs_inverse')
    probs_ready = nc.alloc_semaphore('probs_ready')
    probs_turned = nc.alloc_semaphore('probs_turned')
    probs_turned_copied = nc.alloc_semaphore('probs_turned_copied')
    heads_turned = nc.alloc_semaphore('heads_turned')
    heads_weighed = nc.alloc_semaphore('heads_weighed')
    heads_copied = nc.alloc_semaphore('heads_copied')
    x_updated = nc.alloc_semaphore('x_updated')
    attn_weights_loaded = nc.alloc_semaphore('attn_weights_loaded')
    attn_small_loaded = nc.alloc_semaphore('attn_small_loaded')
    causal_bf16 = nc.alloc_semaphore('causal_bf16')
    batch_copied = nc.alloc_semaphore('batch_copied')
    attn_projected = nc.alloc_semaphore('attn_projected')
    attn_activated = nc.alloc_semaphore('attn_activated')
    alpha_projected = nc.alloc_semaphore('alpha_projected')
    alpha_abs = nc.alloc_semaphore('alpha_abs')
    alpha_exp = nc.alloc_semaphore('alpha_exp')
    alpha_log = nc.alloc_semaphore('alpha_log')
    alpha_positive = nc.alloc_semaphore('alpha_positive')
    alpha_softplus = nc.alloc_semaphore('alpha_softplus')
    log_alpha_ready = nc.alloc_semaphore('log_alpha_ready')
    tail_sums = nc.alloc_semaphore('tail_sums')
    tail_decays = nc.alloc_semaphore('tail_decays')
    chunk_values = nc.alloc_semaphore('chunk_values')
    chunk_values_copied = nc.alloc_semaphore('chunk_values_copied')
    segment_operand = nc.alloc_semaphore('segment_operand')
    segment_sums = nc.alloc_semaphore('segment_sums')
    segment_decays = nc.alloc_semaphore('segment_decays')
    chunk_keys = nc.alloc_semaphore('chunk_keys')
    chunk_keys_decayed = nc.alloc_semaphore('chunk_keys_decayed')
    head_sums = nc.alloc_semaphore('head_sums')
    head_decays = nc.alloc_semaphore('head_decays')
    queries_decayed = nc.alloc_semaphore('queries_decayed')
    chunk_scores = nc.alloc_semaphore('chunk_scores')
    chunk_scores_decayed = nc.alloc_semaphore('chunk_scores_decayed')
    chunk_out = nc.alloc_semaphore('chunk_out')
    chunk_out_copied = nc.alloc_semaphore('chunk_out_copied')
    state_update = nc.alloc_semaphore('state_update')
    state_ready = nc.alloc_semaphore('state_ready')
    state_decayed = nc.alloc_semaphore('state_decayed')
    state_zeroed = nc.alloc_semaphore('state_zeroed')
    norm_stats = nc.alloc_semaphore('norm_stats')
    norm_aggregated = nc.alloc_semaphore('norm_aggregated')
    group_means = nc.alloc_semaphore('group_means')
    mean_offsets = nc.alloc_semaphore('mean_offsets')
    mean_offsets_squared = nc.alloc_semaphore('mean_offsets_squared')
    group_spread = nc.alloc_semaphore('group_spread')
    group_variances = nc.alloc_semaphore('group_variances')
    group_log = nc.alloc_semaphore('group_log')
    group_inverse = nc.alloc_semaphore('group_inverse')
    group_scale = nc.alloc_semaphore('group_scale')
    group_shift = nc.alloc_semaphore('group_shift')
    group_bias = nc.alloc_semaphore('group_bias')
    heads_normed = nc.alloc_semaphore('heads_normed')
    heads_gated = nc.alloc_semaphore('heads_gated')
    attn_out = nc.alloc_semaphore('attn_out')
    ln_input = nc.alloc_semaphore('ln_input')
    ln_mean = nc.alloc_semaphore('ln_mean')
    ln_centred = nc.alloc_semaphore('ln_centred')
    ln_squared = nc.alloc_semaphore('ln_squared')
    ln_variance = nc.alloc_semaphore('ln_variance')
    ln_log = nc.alloc_semaphore('ln_log')
    ln_inverse = nc.alloc_semaphore('ln_inverse')
    ln_done = nc.alloc_semaphore('ln_done')
    ctx_keys = nc.alloc_semaphore('ctx_keys')
    ctx_keys_copied = nc.alloc_semaphore('ctx_keys_copied')
    ctx_folded = nc.alloc_semaphore('ctx_folded')
    ctx_copied = nc.alloc_semaphore('ctx_copied')
    ctx_bias = nc.alloc_semaphore('ctx_bias')
    ctx_values = nc.alloc_semaphore('ctx_values')
    ctx_values_batch = nc.alloc_semaphore('ctx_values_batch')
    cross_logits = nc.alloc_semaphore('cross_logits')
    cross_max = nc.alloc_semaphore('cross_max')
    cross_shifted = nc.alloc_semaphore('cross_shifted')
    cross_exp = nc.alloc_semaphore('cross_exp')
    cross_sum = nc.alloc_semaphore('cross_sum')
    cross_inverse = nc.alloc_semaphore('cross_inverse')
    cross_probs = nc.alloc_semaphore('cross_probs')
    cross_turned = nc.alloc_semaphore('cross_turned')
    cross_turned_copied = nc.alloc_semaphore('cross_turned_copied')
    cross_out = nc.alloc_semaphore('cross_out')
    heads_turned_copied = nc.alloc_semaphore('heads_turned_copied')
    attn_projected_out = nc.alloc_semaphore('attn_projected_out')
    x_plus_attn = nc.alloc_semaphore('x_plus_attn')
    ffn_shifted = nc.alloc_semaphore('ffn_shifted')
    ffn_mean = nc.alloc_semaphore('ffn_mean')
    ffn_centred = nc.alloc_semaphore('ffn_centred')
    ffn_squared = nc.alloc_semaphore('ffn_squared')
    ffn_variance = nc.alloc_semaphore('ffn_variance')
    ffn_log = nc.alloc_semaphore('ffn_log')
    ffn_inverse = nc.alloc_semaphore('ffn_inverse')
    ffn_normed = nc.alloc_semaphore('ffn_normed')
    ffn_input = nc.alloc_semaphore('ffn_input')
    hidden_ready = nc.alloc_semaphore('hidden_ready')
    gate_gelu = nc.alloc_semaphore('gate_gelu')
    hidden_gated = nc.alloc_semaphore('hidden_gated')
    ffn_out = nc.alloc_semaphore('ffn_out')
    out_stored = nc.alloc_semaphore('out_stored')
    HIDDEN_CHUNKS = [128, 128, 85]
    with nc.Block() as block:

        @block.sync
        def _(sp):
            sp.dma_start(x_all[:, :], io['x']).then_inc(x_loaded, 16)
            for w, k in ((w_q, 'a_wq'), (w_k, 'a_wk'), (w_v, 'a_wv'), (w_gate, 'a_wg')):
                sp.dma_start(w[:, :], io[k]).then_inc(attn_weights_loaded, 16)
            sp.dma_start(w_o[:, :, :], io['a_wo'].rearrange('(c p) n -> p c n', p=PARTS)).then_inc(attn_weights_loaded, 16)
            for t, k in ((triangles, 'tri'), (head_mean_w, 'bd'), (norm_affine[:, 0:2, :], 'a_gn'), (w_alpha, 'a_wa'), (b_alpha[0:1, :], 'a_ba'), (ones, 'ones'), (ctx_t, 'ctx'), (w_cross, 'x_w'), (b_cross, 'x_b')):
                sp.dma_start(t, io[k]).then_inc(attn_small_loaded, 16)
            for t, k in ((ident, 'ident'), (mean_w, 'mean_w'), (window_mask, 'mask'), (rotary_base, 'base'), (layer_vecs, 'vec')):
                sp.dma_start(t[:], io[k]).then_inc(constants_loaded, 16)
            for j, k in enumerate(('qs', 'qs_sw', 'ks', 'ks_sw')):
                sp.dma_start(qk_scales[:, j, :, :], io[k].partition_broadcast(PARTS)).then_inc(constants_loaded, 16)
            sp.wait_ge(attn_projected, 24 * BATCHES)
            sp.wait_ge(chunk_values, 4 * BATCHES)
            sp.wait_ge(attn_out, BATCHES)
            sp.dma_start(w_q[:, :], io['wqkv'][0, :, 0:1024]).then_inc(wq_loaded, 16)
            sp.dma_start(w_k[:, :], io['wqkv'][0, :, 1024:2048]).then_inc(wk_loaded, 16)
            sp.dma_start(w_v[:, :], io['wqkv'][0, :, 2048:3072]).then_inc(wv_loaded, 16)

            def ffn_w(l):
                sp.dma_start(w_o[:, :, :], io['wo'][l].rearrange('(c p) n -> p c n', p=PARTS)).then_inc(wo_loaded, 16)

            def w1(l):
                sp.dma_start(w_1[:, :], io['w1'][l]).then_inc(w1_loaded, 16)

            def w2(l):
                sp.dma_start(w_2[:, 0:2, :], io['w2'][l, 0:256, :].rearrange('(c p) n -> p c n', p=PARTS)).then_inc(w2_loaded, 16)
                sp.dma_start(w_2[0:85, 2, :], io['w2'][l, 256:341, :]).then_inc(w2_loaded, 16)
            ffn_w(0)
            w1(0)
            w2(0)
            if LAYERS > 1:
                with sp.Fori(1, LAYERS) as l:
                    sp.wait_ge(q_projected, l * 16)
                    sp.dma_start(w_q[:, :], io['wqkv'][bass.ds(l, 1), :, 0:1024].rearrange('o p n -> (o p) n')).then_inc(wq_loaded, 16)
                    sp.wait_ge(k_projected, l * 16)
                    sp.dma_start(w_k[:, :], io['wqkv'][bass.ds(l, 1), :, 1024:2048].rearrange('o p n -> (o p) n')).then_inc(wk_loaded, 16)
                    sp.wait_ge(values_23, l * 16)
                    sp.dma_start(w_v[:, :], io['wqkv'][bass.ds(l, 1), :, 2048:3072].rearrange('o p n -> (o p) n')).then_inc(wv_loaded, 16)
                    sp.wait_ge(attn_projected_out, l * 4)
                    sp.dma_start(w_o[:, :, :], io['wo'][bass.ds(l, 1)].rearrange('o (c p) n -> p (o c) n', p=PARTS)).then_inc(wo_loaded, 16)
                    sp.wait_ge(hidden_ready, l * 12)
                    sp.dma_start(w_1[:, :], io['w1'][bass.ds(l, 1)].rearrange('o p n -> (o p) n')).then_inc(w1_loaded, 16)
                    sp.wait_ge(ffn_out, l * 4)
                    sp.dma_start(w_2[:, 0:2, :], io['w2'][bass.ds(l, 1), 0:256, :].rearrange('o (c p) n -> p (o c) n', p=PARTS)).then_inc(w2_loaded, 16)
                    sp.dma_start(w_2[0:85, 2, :], io['w2'][bass.ds(l, 1), 256:341, :].rearrange('o p n -> (o p) n')).then_inc(w2_loaded, 16)
            lf = 8
            for b in range(BATCHES):
                sp.wait_ge(ln_done, lf + b + 1)
                sp.dma_start(io['out'][:, b * SEQ:(b + 1) * SEQ], x_all[:, b * SEQ:(b + 1) * SEQ]).then_inc(out_stored, 16)
            sp.wait_ge(out_stored, 16 * BATCHES)

        @block.tensor
        def _(pe):
            mm = nc.tensor.matmul

            def ln(k):
                pe.wait_ge(ln_input, k + 1)
                mm(psum[:, 0, :], mean_w[:, :], normed[:, :], start=True, stop=True).then_inc(ln_mean, 1)
                pe.wait_ge(ln_squared, k + 1)
                mm(psum[:, 1, :], mean_w[:, :], spread[:, :], start=True, stop=True).then_inc(ln_variance, 1)

            def ab(b):
                pe.wait_ge(batch_copied, b + 1)
                for t in range(24):
                    w = (w_q, w_k, w_gate)[t // 8]
                    c = t % 8
                    if t >= 4:
                        if due(b * 24 + t - 3):
                            pe.wait_ge(attn_activated, b * 24 + t - 3)
                    if t < 4:
                        if due(2 * b):
                            pe.wait_ge(ln_done, 2 * b)
                    mm(psum[:, t % 4, :], w[:, c * 128:c * 128 + 128], x_batch[:, :], start=True, stop=True).then_inc(attn_projected, 1)
                for n in range(4):
                    mm(psum[:, 4, n * 16:n * 16 + 16], x_batch[:, n * 128:n * 128 + 128], w_alpha, start=n == 0, stop=False, skip_group_check=True)
                    m = mm(psum[:, 4, n * 16:n * 16 + 16], ones[0:1, :], b_alpha[0:1, :], start=False, stop=True, skip_group_check=True)
                m.then_inc(alpha_projected, 1)
                pe.wait_ge(log_alpha_ready, b + 1)
                mm(psum[:, 5, 0:64], triangles[:, 1, :], log_alpha, start=True, stop=True).then_inc(tail_sums, 1)
                pe.wait_ge(tail_decays, b + 1)
                pe.wait_ge(attn_activated, b * 24 + 24)
                for n in range(4):
                    k = 4 * b + n
                    xc = x_batch[:, n * 128:n * 128 + 128]
                    nn = slice(n * 128, n * 128 + 128)
                    if due(k):
                        pe.wait_ge(state_ready, k)
                    for h in range(2):
                        m = mm(psum[:, 4 + h, :], xc, w_v[:, h * 512:h * 512 + 512], start=True, stop=True)
                    m.then_inc(chunk_values, 1)
                    pe.wait_ge(segment_operand, k + 1)
                    if due(k):
                        pe.wait_ge(chunk_scores_decayed, k)
                    for j in range(4):
                        mm(psum[:, j, :], ident_bf16[:, :], causal_bf16_mask[:, :].unsqueeze(1).broadcast_to([PARTS, 4, 128]), start=True, stop=False)
                        m = mm(psum[:, j, :], triangles[:, 1, :], seg_operand[:, 4 * j:4 * j + 4, :], start=False, stop=True)
                    m.then_inc(segment_sums, 1)
                    if due(k):
                        pe.wait_ge(chunk_out_copied, k)
                    for c in range(8):
                        m = nc.tensor.transpose(psum[:, 6 + c // 4, c % 4 * 128:c % 4 * 128 + 128], k_act[:, c, nn], ident[:, :])
                    m.then_inc(chunk_keys, 1)
                    pe.wait_ge(chunk_values_copied, k + 1)
                    for c in range(8):
                        for q in range(2):
                            m = mm(psum[64 * q:64 * q + 64, 4 + c // 4, c % 4 * 128:c % 4 * 128 + 128], log_alpha[:, n * 16 + 2 * c + q:n * 16 + 2 * c + q + 1].broadcast_to([PARTS, 64]), triangles[:, 0, :], start=True, stop=True)
                    m.then_inc(head_sums, 1)
                    pe.wait_ge(segment_decays, k + 1)
                    for q in range(2):
                        for c in range(8):
                            m = mm(psum[:, 2 * q + c // 4, c % 4 * 128:c % 4 * 128 + 128], k_act[64 * q:64 * q + 64, c, nn], q_act[64 * q:64 * q + 64, c, nn], start=True, stop=True)
                    m.then_inc(chunk_scores, 1)
                    pe.wait_ge(chunk_keys_decayed, k + 1)
                    pe.wait_ge(chunk_scores_decayed, k + 1)
                    pe.wait_ge(queries_decayed, k + 1)
                    if due(k):
                        pe.wait_ge(state_ready, k)
                    pe.wait_ge(state_zeroed, b + 1)
                    for c in range(8):
                        for q in range(2):
                            o = psum[64 * q:64 * q + 64, 6 + c // 4, c % 4 * 128:c % 4 * 128 + 128]
                            mm(o, v_chunk[:, c * 128 + q * 64:c * 128 + q * 64 + 64], pair_scores[:, q * 8 + c, :], start=True, stop=False, skip_group_check=True)
                            m = mm(o, state[64 * q:64 * q + 64, c, :], q_decayed[64 * q:64 * q + 64, c, :], start=False, stop=True, skip_group_check=True)
                    m.then_inc(chunk_out, 1)
                    pe.wait_ge(head_decays, k + 1)
                    for c in range(8):
                        for q in range(2):
                            m = mm(psum[64 * q:64 * q + 64, 4, c * 64:c * 64 + 64], k_decayed[:, c * 128 + q * 64:c * 128 + q * 64 + 64], v_chunk[:, c * 128 + q * 64:c * 128 + q * 64 + 64], start=True, stop=True)
                    m.then_inc(state_update, 1)
                pe.wait_ge(norm_aggregated, b + 1)
                mm(psum[:, 0, 0:8], head_mean_w, chan_mean_var[:, :, 0], start=True, stop=True).then_inc(group_means, 1)
                pe.wait_ge(group_spread, b + 1)
                mm(psum[:, 1, 0:8], head_mean_w, group_vars[:, 0, :], start=True, stop=True).then_inc(group_variances, 1)
                for c in range(8):
                    pe.wait_ge(heads_gated, 8 * b + c + 1)
                    m = mm(psum[:, 2, :], w_o[:, c, :], attn_heads[:, c, :], start=c == 0, stop=c == 7)
                m.then_inc(attn_out, 1)
                ln(2 * b)
                pe.wait_ge(ln_done, 2 * b + 1)
                for n in range(4):
                    mm(psum[:, 3, n * 32:n * 32 + 32], x_batch[:, n * 128:n * 128 + 128], ctx_k_folded[:, bass.ds(b * 32, 32)], start=n == 0, stop=False, skip_group_check=True)
                    m = mm(psum[:, 3, n * 32:n * 32 + 32], ones[0:1, :], ctx_k_bias[0:1, bass.ds(b * 32, 32)], start=False, stop=True, skip_group_check=True)
                m.then_inc(cross_logits, 1)
                pe.wait_ge(cross_probs, b + 1)
                for n in range(4):
                    m = nc.tensor.transpose(psum[0:32, 4, n * 128:n * 128 + 128], cross_p[:, n, :], ident[:, :])
                m.then_inc(cross_turned, 1)
                pe.wait_ge(cross_turned_copied, b + 1)
                pe.wait_ge(ctx_values_batch, b + 1)
                mm(psum[:, 5, :], ctx_v_batch[0:32, :], cross_p_t[0:32, :], start=True, stop=True).then_inc(cross_out, 1)
                ln(2 * b + 1)

            def cross_setup():
                pe.wait_ge(attn_small_loaded, 16 * 9)
                mm(psum[:, 0, 0:128], w_cross[:, 0, :], ctx_t, start=True, stop=True).then_inc(ctx_keys, 1)
                pe.wait_ge(ctx_keys_copied, 1)
                mm(psum[:, 1, 0:128], w_cross[:, 1, :], ctx_k, start=True, stop=True).then_inc(ctx_folded, 1)
                mm(psum[0:1, 2, 0:128], b_cross[:, 0:1], ctx_k, start=True, stop=True).then_inc(ctx_bias, 1)
                for b in range(4):
                    m = mm(psum[0:32, 3, b * 128:b * 128 + 128], ctx_t[:, b * 32:b * 32 + 32], w_cross[:, 2, :], start=True, stop=True)
                m.then_inc(ctx_values, 1)
                pe.wait_ge(ctx_copied, 3)

            def step(g, n, it, a, b, c):
                par0 = (n - 1) % 2
                nb = (n - 1) % 4
                ffn = it is not None

                def project(R, w, half):
                    return mm(R[:, half, :], x_shift[:, 32 + n * 128:32 + n * 128 + 128], w[:, half * 512:half * 512 + 512], start=True, stop=True)

                def scores(pairs):
                    for c8 in pairs:
                        for q in range(2):
                            for w in range(4):
                                kc = 32 + 128 * par0 + 32 * (w - 1)
                                m = mm(psum_a[32 * w:32 * w + 32, q, c8 * 64:c8 * 64 + 64], q_t[64 * q:64 * q + 64, c8, 32 * w:32 * w + 32], k_t[64 * q:64 * q + 64, c8, kc:kc + 64], start=True, stop=True)
                    return m

                def values(half):
                    for w in range(2):
                        if half == 0 and w == 1 and c:
                            if b:
                                if due(g):
                                    pe.wait_ge(scores_masked, g)
                            if due(g - 1):
                                pe.wait_ge(values_23_copied, g - 1)
                        col = nb * 128 + (2 * half + w) * 32
                        for par in range(2):
                            m = mm(psum_b[64 * par:64 * par + 64, w, :].rearrange('p (c d) -> p c d', d=64), x_shift[:, col:col + 64], w_v[:, :].rearrange('p (c q d) -> p q c d', q=2, d=64)[:, par], start=True, stop=True)
                    m.then_inc(values_01 if half == 0 else values_23, 1)

                def weigh(pairs):
                    for c8 in pairs:
                        for q in range(2):
                            for w in range(4):
                                m = mm(psum_a[32 * w:32 * w + 32, q, c8 * 64:c8 * 64 + 64], probs_t[64 * q:64 * q + 64, c8, 32 * w:32 * w + 32], v_win[64 * q:64 * q + 64, n % 2, w, c8 * 64:c8 * 64 + 64], start=True, stop=True)
                    return m

                def hid(k):
                    R = (q_psum, k_psum, q_psum)[k]
                    M = HIDDEN_CHUNKS[k]
                    mm(R[0:M, 0, :], w_1[:, k * 128:k * 128 + M], ffn_in[:, :], start=True, stop=True)
                    mm(R[0:M, 1, :], w_1[:, 341 + k * 128:341 + k * 128 + M], ffn_in[:, :], start=True, stop=True).then_inc(hidden_ready, 1)
                if b:
                    if due(g):
                        pe.wait_ge(q_normed, g)
                    if c:
                        if due(g - 2):
                            pe.wait_ge(heads_copied, g - 2)
                    for t in range(8):
                        m = nc.tensor.transpose(flat(psum_a)[:, t * 128:t * 128 + 128], qk_norm[:, 0, t * 128:t * 128 + 128], ident[:, :])
                    m.then_inc(q_turned, 1)
                    if due(g):
                        pe.wait_ge(k_normed, g)
                    if due(g - 2):
                        pe.wait_ge(heads_turned_copied, g - 2)
                    if isinstance(g, int) and g < 3:
                        if due(g - 1):
                            pe.wait_ge(values_23_copied, g - 1)
                    for t in range(8):
                        m = nc.tensor.transpose(flat(psum_b)[:, t * 128:t * 128 + 128], qk_norm[:, 1, t * 128:t * 128 + 128], ident[:, :])
                    m.then_inc(k_turned, 1)
                if a:
                    if due(2 * (g + 1)):
                        pe.wait_ge(block_shifted, 2 * (g + 1))
                    if due(16 * (g // 16 + 1)):
                        pe.wait_ge(wq_loaded, 16 * (g // 16 + 1))
                    if due(g):
                        pe.wait_ge(q_sin, g)
                    if due(g):
                        pe.wait_ge(q_squared, g)
                    if ffn and n == 0:
                        if due(3 * it):
                            pe.wait_ge(hidden_gated, 3 * it)
                    if ffn and n == 3:
                        pe.wait_ge(ffn_log, it + 1)
                    project(q_psum, w_q, 0)
                    project(q_psum, w_q, 1).then_inc(q_projected, 1)
                if c:
                    if due(g - 1):
                        pe.wait_ge(probs_ready, g - 1)
                    if b:
                        if due(g):
                            pe.wait_ge(k_turned_copied, g)
                    else:
                        if due(g - 2):
                            pe.wait_ge(heads_turned_copied, g - 2)
                        if due(g - 2):
                            pe.wait_ge(heads_copied, g - 2)
                    for t in range(8):
                        m = nc.tensor.transpose(flat(psum_b)[:, t * 128:t * 128 + 128], probs[:, t, :, :].rearrange('p a b -> p (a b)'), ident[:, :])
                    m.then_inc(probs_turned, 1)
                if a:
                    if due(16 * (g // 16 + 1)):
                        pe.wait_ge(wk_loaded, 16 * (g // 16 + 1))
                    if due(g):
                        pe.wait_ge(k_sin, g)
                    if due(g):
                        pe.wait_ge(k_squared, g)
                    if ffn and n == 0:
                        pe.wait_ge(x_updated, it + 4)
                    if b:
                        if due(g):
                            pe.wait_ge(q_turned_copied, g)
                        if due(g):
                            pe.wait_ge(k_turned_copied, g)
                    project(k_psum, w_k, 0)
                if b:
                    if not a:
                        if due(g):
                            pe.wait_ge(q_turned_copied, g)
                        if due(g):
                            pe.wait_ge(k_turned_copied, g)
                    scores(range(0, 4))
                if a:
                    project(k_psum, w_k, 1).then_inc(k_projected, 1)
                if b:
                    scores(range(4, 8)).then_inc(scores_ready, 1)
                if ffn and n == 2:
                    if due(16 * (it // 4 + 1)):
                        pe.wait_ge(wo_loaded, 16 * (it // 4 + 1))
                    pe.wait_ge(heads_turned_copied, 4 * it + 4)
                    if a:
                        pe.wait_ge(q_sin, g + 1)
                        pe.wait_ge(q_squared, g + 1)
                    for k in range(8):
                        m = mm(q_psum[:, 0, :], w_o[:, k, :], heads_t[:, k, :], start=k == 0, stop=k == 7)
                    m.then_inc(attn_projected_out, 1)
                if ffn and n == 3:
                    if due(16 * (it // 4 + 1)):
                        pe.wait_ge(w1_loaded, 16 * (it // 4 + 1))
                    pe.wait_ge(ffn_input, it + 1)
                    if a:
                        pe.wait_ge(q_sin, g + 1)
                        pe.wait_ge(q_squared, g + 1)
                    hid(0)
                if b:
                    if due(16 * ((g - 1) // 16 + 1)):
                        pe.wait_ge(wv_loaded, 16 * ((g - 1) // 16 + 1))
                    if c:
                        if due(g - 1):
                            pe.wait_ge(probs_turned_copied, g - 1)
                    values(0)
                if ffn and n == 3:
                    if a:
                        pe.wait_ge(k_sin, g + 1)
                        pe.wait_ge(k_squared, g + 1)
                    hid(1)
                if c:
                    if not b:
                        if due(g - 1):
                            pe.wait_ge(probs_turned_copied, g - 1)
                        if due(g - 1):
                            pe.wait_ge(values_23_copied, g - 1)
                    weigh(range(0, 4))
                if b:
                    if due(g):
                        pe.wait_ge(values_01_copied, g)
                    values(1)
                if ffn and n == 3:
                    pe.wait_ge(hidden_gated, 3 * it + 1)
                    hid(2)
                if c:
                    weigh(range(4, 8)).then_inc(heads_weighed, 1)
                if ffn and n == 2:
                    pe.wait_ge(ffn_shifted, 2 * it + 2)
                    mm(q_psum[:, 1, :], mean_w[:, :], ffn_x[:, :], start=True, stop=True).then_inc(ffn_mean, 1)
                if c:
                    if due(g - 1):
                        pe.wait_ge(heads_copied, g - 1)
                    if b:
                        if due(g):
                            pe.wait_ge(values_23_copied, g)
                    for t in range(8):
                        m = nc.tensor.transpose(flat(psum_b)[:, t * 128:t * 128 + 128], heads[:, t * 128:t * 128 + 128], ident[:, :])
                    m.then_inc(heads_turned, 1)
                if ffn and n == 2:
                    pe.wait_ge(ffn_squared, it + 1)
                    mm(q_psum[:, 0, :], mean_w[:, :], spread[:, :], start=True, stop=True).then_inc(ffn_variance, 1)
                if ffn and n == 3:
                    pe.wait_ge(hidden_gated, 3 * it + 3)
                    if due(32 * (it // 4 + 1)):
                        pe.wait_ge(w2_loaded, 32 * (it // 4 + 1))
                    for k in range(3):
                        m = mm(k_psum[:, 0, :], w_2[0:HIDDEN_CHUNKS[k], k, :], hidden[0:HIDDEN_CHUNKS[k], k, :], start=k == 0, stop=k == 2)
                    m.then_inc(ffn_out, 1)
            pe.wait_ge(constants_loaded, 16 * 9)
            pe.wait_ge(attn_weights_loaded, 16 * 5)
            pe.wait_ge(attn_small_loaded, 16 * 9)
            pe.wait_ge(causal_bf16, 2)
            cross_setup()
            ab(0)
            with pe.Fori(1, BATCHES) as b:
                ab(b)
            pe.wait_ge(ln_done, 8)
            for g in range(4):
                step(g, g, None, True, g >= 1, g >= 2)
            for n in range(4):
                step(4 + n, n, 0, True, True, True)
            if FFN_PASSES > 2:
                with pe.Fori(1, FFN_PASSES - 1) as it:
                    for n in range(4):
                        step(it * 4 + (4 + n), n, it, True, True, True)
            for n in range(4):
                step(ALL_BLOCKS + n, n, FFN_PASSES - 1, False, n < 1, n < 2)
            for b in range(4):
                pe.wait_ge(x_updated, FFN_PASSES + 4)
                ln(8 + b)

        @block.scalar
        def _(act):
            A = nc.scalar.activation
            LNEXP = 'natural_log_exp_and_others'
            nc.scalar.preload_act_table_set(LNEXP)

            def ln(k):
                act.wait_ge(ln_centred, k + 1)
                A(spread[:, :], centred[:, :], ACT.Square).then_inc(ln_squared, 1)
                act.wait_ge(ln_variance, k + 1)
                A(spread[:, :], psum[:, 1, :], ACT.Ln, bias=tiny[:, 0:1]).then_inc(ln_log, 1)
                act.wait_ge(ln_log, k + 1)
                A(spread[:, :], spread[:, :], ACT.Exp, scale=-0.5).then_inc(ln_inverse, 1)

            def ab(b):
                if due(8 * b):
                    act.wait_ge(heads_gated, 8 * b)
                for t in range(24):
                    act.wait_ge(attn_projected, 24 * b + t + 1)
                    if t == 0:
                        if due(4 * b):
                            act.wait_ge(chunk_scores, 4 * b)
                    if t == 8:
                        if due(4 * b):
                            act.wait_ge(chunk_keys, 4 * b)
                    A((q_act, k_act, gate_act)[t // 8][:, t % 8, :], psum[:, t % 4, :], ACT.Silu if t < 16 else ACT.Sigmoid).then_inc(attn_activated, 1)
                nc.scalar.preload_act_table_set(LNEXP)
                act.wait_ge(alpha_projected, b + 1)
                A(alpha_tmp, psum[:, 4, 0:64], ACT.Abs).then_inc(alpha_abs, 1)
                act.wait_ge(alpha_abs, b + 1)
                A(alpha_tmp, alpha_tmp, ACT.Exp, scale=-1.0).then_inc(alpha_exp, 1)
                act.wait_ge(alpha_exp, b + 1)
                A(alpha_tmp, alpha_tmp, ACT.Ln, bias=1.0).then_inc(alpha_log, 1)
                act.wait_ge(tail_sums, b + 1)
                A(tail_decay.rearrange('p a b -> p (a b)'), psum[:, 5, 0:64], ACT.Exp).then_inc(tail_decays, 1)
                for n in range(4):
                    k = 4 * b + n
                    act.wait_ge(chunk_values, k + 1)
                    if due(k):
                        act.wait_ge(state_update, k)
                    A(v_chunk, flat(psum[:, 4:6, :]), ACT.Copy).then_inc(chunk_values_copied, 1)
                    act.wait_ge(segment_sums, k + 1)
                    if due(k):
                        act.wait_ge(chunk_scores_decayed, k)
                    for j in range(2):
                        m = A(pair_decay[:, 8 * j:8 * j + 8, :], psum[:, 2 * j:2 * j + 2, :].rearrange('p a (b c) -> p (a b) c', c=128), ACT.Exp)
                    m.then_inc(segment_decays, 1)
                    act.wait_ge(head_sums, k + 1)
                    if due(k):
                        act.wait_ge(state_ready, k)
                    A(head_decay, psum[:, 4:6, :].rearrange('p a (b c) -> p (a b) c', c=128), ACT.Exp).then_inc(head_decays, 1)
                    act.wait_ge(chunk_out, k + 1)
                    if n == 0:
                        if due(b):
                            act.wait_ge(attn_out, b)
                    A(attn_heads[:, :, n * 128:n * 128 + 128], psum[:, 6:8, :].rearrange('p a (b c) -> p (a b) c', c=128), ACT.Copy).then_inc(chunk_out_copied, 1)
                act.wait_ge(group_variances, b + 1)
                A(group_vars[:, 1, :], psum[:, 1, 0:8], ACT.Ln, bias=tiny[:, 0:1]).then_inc(group_log, 1)
                act.wait_ge(group_log, b + 1)
                A(group_vars[:, 1, :], group_vars[:, 1, :], ACT.Exp, scale=-0.5).then_inc(group_inverse, 1)
                ln(2 * b)
                act.wait_ge(cross_shifted, b + 1)
                A(cross_p, cross_p, ACT.Exp, scale=1 / 32).then_inc(cross_exp, 1)
                ln(2 * b + 1)

            def step(g, n, it, a, b, c):
                ffn = it is not None
                if b:
                    if due(g):
                        act.wait_ge(q_turned, g)
                    if due(g - 1):
                        act.wait_ge(scores_ready, g - 1)
                    A(q_t[:, :, :], flat(psum_a).rearrange('p (c t) -> p c t', t=128), ACT.Copy).then_inc(q_turned_copied, 1)
                    if due(g):
                        act.wait_ge(k_turned, g)
                    par = (n - 1) % 2
                    src = flat(psum_b).rearrange('p (c t) -> p c t', t=128)
                    if par == 1:
                        A(k_t[:, :, 0:32], src[:, :, 96:128], ACT.Copy)
                    A(k_t[:, :, 32 + 128 * par:160 + 128 * par], src, ACT.Copy).then_inc(k_turned_copied, 1)
                if ffn and n == 3:
                    act.wait_ge(ffn_normed, it + 1)
                    A(ffn_in[:, :], normed[:, :], ACT.Identity, scale=layer_vecs[:, bass.ds(it // 4 * 9 + 6, 1)], bias=layer_vecs[:, bass.ds(it // 4 * 9 + 7, 1)]).then_inc(ffn_input, 1)
                if a:
                    act.wait_ge(q_projected, g + 1)
                    if due(g):
                        act.wait_ge(q_sums, g)
                    A(squares[:, 0, :], flat(q_psum), ACT.Square).then_inc(q_squared, 1)
                if c:
                    if due(g - 1):
                        act.wait_ge(probs_turned, g - 1)
                    if due(g - 2):
                        act.wait_ge(heads_weighed, g - 2)
                    A(probs_t[:, :, :], flat(psum_b).rearrange('p (c t) -> p c t', t=128), ACT.Copy).then_inc(probs_turned_copied, 1)
                if a:
                    act.wait_ge(k_projected, g + 1)
                    if due(g):
                        act.wait_ge(k_sums, g)
                    A(squares[:, 1, :], flat(k_psum), ACT.Square).then_inc(k_squared, 1)
                if b:
                    pv = (n - 1) % 2
                    if due(g):
                        act.wait_ge(values_01, g)
                    if due(g - 2):
                        act.wait_ge(heads_weighed, g - 2)
                    A(v_win[:, pv, 0:2, :], psum_b, ACT.Copy).then_inc(values_01_copied, 1)
                if a:
                    act.wait_ge(sums_clamped, g + 1)
                    A(norm_logs[:, :], sq_clamped[:, :], ACT.Ln).then_inc(norms_log, 1)
                    act.wait_ge(norms_log, g + 1)
                    if due(g):
                        act.wait_ge(k_normed, g)
                    A(inv_norms[:, :, :].rearrange('p a b -> p (a b)'), norm_logs[:, :], ACT.Exp, scale=-0.5).then_inc(inverse_norms, 1)

                def gelu(k):
                    M = HIDDEN_CHUNKS[k]
                    R = (q_psum, k_psum, q_psum)[k]
                    act.wait_ge(hidden_ready, 3 * it + k + 1)
                    if k == 0:
                        if due(3 * it):
                            act.wait_ge(hidden_gated, 3 * it)
                    A(gate[0:M, k, :], R[0:M, 1, :], ACT.Gelu, bias=layer_vecs[0:M, bass.ds(it // 4 * 9 + 3 + k, 1)]).then_inc(gate_gelu, 1)
                if ffn and n == 2:
                    act.wait_ge(x_plus_attn, it + 1)
                    if due(it):
                        act.wait_ge(ffn_centred, it)
                    xo = it % 4 * 512
                    A(ffn_x[0:64, :], x_all[0:64, bass.ds(xo, 512)], ACT.Copy).then_inc(ffn_shifted, 1)
                    A(ffn_x[64:128, 1:512], x_all[64:128, bass.ds(xo, 511)], ACT.Copy).then_inc(ffn_shifted, 1)
                if ffn and n == 3:
                    gelu(0)
                    gelu(1)
                if b:
                    if due(g):
                        act.wait_ge(values_23, g)
                    A(v_win[:, pv, 2:4, :], psum_b, ACT.Copy).then_inc(values_23_copied, 1)
                if ffn and n == 3:
                    gelu(2)
                    nc.scalar.preload_act_table_set(LNEXP)
                if b:
                    if due(g):
                        act.wait_ge(scores_shifted, g)
                    if due(g - 1):
                        act.wait_ge(probs_turned, g - 1)
                    A(probs[:, :, :, :], scores_sb[:, :, :, :], ACT.Exp).then_inc(probs_exp, 1)
                if ffn and n == 2:
                    act.wait_ge(ffn_centred, it + 1)
                    A(spread[:, :], centred[:, :], ACT.Square).then_inc(ffn_squared, 1)
                if c:
                    if due(g - 1):
                        act.wait_ge(heads_weighed, g - 1)
                    if due(g - 2):
                        act.wait_ge(heads_turned, g - 2)
                    A(heads.rearrange('p (c q d) -> p q c d', q=2, d=64), psum_a.rearrange('p q (c d) -> p q c d', d=64), ACT.Copy).then_inc(heads_copied, 1)
                    if due(g - 1):
                        act.wait_ge(heads_turned, g - 1)
                    nn = (n - 2) % 4
                    if nn == 0:
                        if due((g - 2) // 4):
                            act.wait_ge(attn_projected_out, (g - 2) // 4)
                    A(heads_t[:, :, nn * 128:nn * 128 + 128], flat(psum_b).rearrange('p (c t) -> p c t', t=128), ACT.Copy).then_inc(heads_turned_copied, 1)
                if ffn and n == 2:
                    act.wait_ge(ffn_variance, it + 1)
                    A(spread[:, :], q_psum[:, 0, :], ACT.Ln, bias=tiny[:, 0:1]).then_inc(ffn_log, 1)
                    act.wait_ge(ffn_log, it + 1)
                    A(spread[:, :], spread[:, :], ACT.Exp, scale=-0.5).then_inc(ffn_inverse, 1)
            act.wait_ge(constants_loaded, 16 * 9)
            act.wait_ge(zeroed, 5)
            ab(0)
            with act.Fori(1, BATCHES) as b:
                ab(b)
            for g in range(4):
                step(g, g, None, True, g >= 1, g >= 2)
            for n in range(4):
                step(4 + n, n, 0, True, True, True)
            if FFN_PASSES > 2:
                with act.Fori(1, FFN_PASSES - 1) as it:
                    for n in range(4):
                        step(it * 4 + (4 + n), n, it, True, True, True)
            for n in range(4):
                step(ALL_BLOCKS + n, n, FFN_PASSES - 1, False, n < 1, n < 2)
            for b in range(4):
                ln(8 + b)

        @block.vector
        def _(dve):
            V = nc.vector
            h16 = lambda ap: ap.rearrange('p (h d) -> p h d', d=64)

            def step(g, n, it, a, b, c):
                ffn = it is not None
                if ffn and n == 3:
                    dve.wait_ge(ffn_inverse, it + 1)
                    V.tensor_tensor(normed[:, :], centred[:, :], spread[:, :], ALU.mult).then_inc(ffn_normed, 1)
                if a and n == 0:
                    ly = g // 16
                    for j in range(4):
                        t = V.tensor_tensor(rotary_tab[:, j, :, :], rotary_base[:, j, :, :], qk_scales[:, j, bass.ds(ly, 1), :].broadcast_to([PARTS, 4, 64]), ALU.mult)
                    t.then_inc(tables_scaled, 1)
                if a:
                    dve.wait_ge(tables_scaled, g // 4 + 1)
                    dve.wait_ge(q_squared, g + 1)
                    if due(g):
                        dve.wait_ge(q_normed, g)
                    src = h16(flat(q_psum))
                    V.tensor_tensor(h16(cos_part[:, 0, :]), src, rotary_tab[:, 2 * 0, n, :].unsqueeze(1).broadcast_to([PARTS, 16, 64]), ALU.mult).then_inc(q_cos, 1)
                    if due(g):
                        dve.wait_ge(q_rotated, g)
                    V.tensor_tensor(h16(sin_part[:, 0, :])[:, :, 0:32], src[:, :, 32:64], rotary_tab[:, 2 * 0 + 1, n, 0:32].unsqueeze(1).broadcast_to([PARTS, 16, 32]), ALU.mult)
                    V.tensor_tensor(h16(sin_part[:, 0, :])[:, :, 32:64], src[:, :, 0:32], rotary_tab[:, 2 * 0 + 1, n, 32:64].unsqueeze(1).broadcast_to([PARTS, 16, 32]), ALU.mult).then_inc(q_sin, 1)
                    if due(g):
                        dve.wait_ge(sums_clamped, g)
                    V.tensor_reduce(sq_sums[:, 0, :], h16(squares[:, 0, :]), AX, ALU.add).then_inc(q_sums, 1)
                    dve.wait_ge(k_squared, g + 1)
                    if due(g):
                        dve.wait_ge(k_normed, g)
                    src = h16(flat(k_psum))
                    V.tensor_tensor(h16(cos_part[:, 1, :]), src, rotary_tab[:, 2 * 1, n, :].unsqueeze(1).broadcast_to([PARTS, 16, 64]), ALU.mult).then_inc(k_cos, 1)
                    if due(g):
                        dve.wait_ge(k_rotated, g)
                    V.tensor_tensor(h16(sin_part[:, 1, :])[:, :, 0:32], src[:, :, 32:64], rotary_tab[:, 2 * 1 + 1, n, 0:32].unsqueeze(1).broadcast_to([PARTS, 16, 32]), ALU.mult)
                    V.tensor_tensor(h16(sin_part[:, 1, :])[:, :, 32:64], src[:, :, 0:32], rotary_tab[:, 2 * 1 + 1, n, 32:64].unsqueeze(1).broadcast_to([PARTS, 16, 32]), ALU.mult).then_inc(k_sin, 1)
                    if b:
                        if due(g):
                            dve.wait_ge(scores_ready, g)
                        if due(g - 1):
                            dve.wait_ge(probs_exp, g - 1)
                        mk = window_mask[:, 0 if (n - 1) % 4 == 0 else 1, :].unsqueeze(1).unsqueeze(1).broadcast_to([PARTS, 2, 8, 64])
                        V.tensor_tensor(scores_sb[:, :, :, :].rearrange('p c q k -> p q c k'), psum_a.rearrange('p q (c k) -> p q c k', k=64), mk, ALU.add).then_inc(scores_masked, 1)
                    V.tensor_reduce(sq_sums[:, 1, :], h16(squares[:, 1, :]), AX, ALU.add).then_inc(k_sums, 1)
                    dve.wait_ge(q_sums, g + 1)
                    dve.wait_ge(k_sums, g + 1)
                    if due(g):
                        dve.wait_ge(norms_log, g)
                    V.tensor_scalar(sq_clamped[:, :], sq_sums[:, :, :].rearrange('p a b -> p (a b)'), 1e-24, None, ALU.max).then_inc(sums_clamped, 1)
                if b and (not a):
                    if due(g):
                        dve.wait_ge(scores_ready, g)
                    if due(g - 1):
                        dve.wait_ge(probs_exp, g - 1)
                    mk = window_mask[:, 0 if (n - 1) % 4 == 0 else 1, :].unsqueeze(1).unsqueeze(1).broadcast_to([PARTS, 2, 8, 64])
                    V.tensor_tensor(scores_sb[:, :, :, :].rearrange('p c q k -> p q c k'), psum_a.rearrange('p q (c k) -> p q c k', k=64), mk, ALU.add).then_inc(scores_masked, 1)
                if ffn and n == 2:
                    dve.wait_ge(attn_projected_out, it + 1)
                    xc = x_all[:, bass.ds(it % 4 * 512, 512)]
                    V.tensor_tensor(xc, q_psum[:, 0, :], xc, ALU.add).then_inc(x_plus_attn, 1)
                if b:
                    if due(g):
                        dve.wait_ge(scores_masked, g)
                    V.tensor_reduce(row_max[:, :].rearrange('p (c q) -> p c q', q=2), scores_sb[:, :, :, :], AX, ALU.max).then_inc(scores_max, 1)
                    if due(g):
                        dve.wait_ge(scores_max, g)
                    s3 = scores_sb[:, :, :, :].rearrange('p c q k -> p (c q) k')
                    V.tensor_tensor(s3, s3, row_max[:, :].unsqueeze(2).broadcast_to([PARTS, 16, 64]), ALU.subtract).then_inc(scores_shifted, 1)

                def hh(k):
                    M = HIDDEN_CHUNKS[k]
                    R = (q_psum, k_psum, q_psum)[k]
                    dve.wait_ge(gate_gelu, 3 * it + k + 1)
                    if k == 0:
                        if due(it):
                            dve.wait_ge(ffn_out, it)
                    V.scalar_tensor_tensor(out=hidden[0:M, k, :], in0=R[0:M, 0, :], scalar=layer_vecs[0:M, bass.ds(it // 4 * 9 + k, 1)], in1=gate[0:M, k, :], op0=ALU.add, op1=ALU.mult).then_inc(hidden_gated, 1)
                if ffn and n == 3:
                    hh(0)
                if a:
                    dve.wait_ge(q_rotated, g + 1)
                    dve.wait_ge(inverse_norms, g + 1)
                    if due(g):
                        dve.wait_ge(q_turned, g)
                    V.tensor_tensor(h16(qk_norm[:, 0, :]), h16(cos_part[:, 0, :]), inv_norms[:, 0, :].unsqueeze(2).broadcast_to([PARTS, 16, 64]), ALU.mult).then_inc(q_normed, 1)
                    if ffn and n == 3:
                        hh(1)
                    dve.wait_ge(k_rotated, g + 1)
                    dve.wait_ge(inverse_norms, g + 1)
                    if due(g):
                        dve.wait_ge(k_turned, g)
                    V.tensor_tensor(h16(qk_norm[:, 1, :]), h16(cos_part[:, 1, :]), inv_norms[:, 1, :].unsqueeze(2).broadcast_to([PARTS, 16, 64]), ALU.mult).then_inc(k_normed, 1)
                elif ffn and n == 3:
                    hh(1)
                if ffn and n == 2:
                    dve.wait_ge(ffn_mean, it + 1)
                    if due(it):
                        dve.wait_ge(ffn_normed, it)
                    V.tensor_tensor(centred[:, :], ffn_x[:, :], q_psum[:, 1, :], ALU.subtract).then_inc(ffn_centred, 1)
                if ffn and n == 3:
                    hh(2)
                if b:
                    if due(g):
                        dve.wait_ge(probs_exp, g)
                    V.tensor_reduce(row_sum[:, :].rearrange('p (c q) -> p c q', q=2), probs[:, :, :, :], AX, ALU.add).then_inc(probs_sum, 1)
                    if due(g):
                        dve.wait_ge(probs_sum, g)
                    if due(g - 1):
                        dve.wait_ge(probs_ready, g - 1)
                    V.reciprocal(row_inv[:, :], row_sum[:, :]).then_inc(probs_inverse, 1)
                if ffn and n == 3:
                    dve.wait_ge(ffn_out, it + 1)
                    xc = x_all[:, bass.ds(it % 4 * 512, 512)]
                    V.scalar_tensor_tensor(out=xc, in0=k_psum[:, 0, :], scalar=layer_vecs[:, bass.ds(it // 4 * 9 + 8, 1)], in1=xc, op0=ALU.add, op1=ALU.add).then_inc(x_updated, 1)

            def ln(k, dst, dst2=None):
                dve.wait_ge(ln_mean, k + 1)
                V.tensor_tensor(centred[:, :], normed[:, :], psum[:, 0, :], ALU.subtract).then_inc(ln_centred, 1)
                dve.wait_ge(ln_inverse, k + 1)
                V.tensor_tensor(dst, centred[:, :], spread[:, :], ALU.mult).then_inc(ln_done, 1)

            def ab(b):
                V.tensor_copy(x_batch[:, :], x_all[:, bass.ds(b * 512, 512)]).then_inc(batch_copied, 1)
                V.memset(state, 0.0).then_inc(state_zeroed, 1)
                dve.wait_ge(alpha_projected, b + 1)
                dve.wait_ge(alpha_abs, b + 1)
                V.tensor_scalar(alpha_soft, psum[:, 4, 0:64], 0.0, None, ALU.max).then_inc(alpha_positive, 1)
                dve.wait_ge(alpha_positive, b + 1)
                dve.wait_ge(alpha_log, b + 1)
                V.tensor_tensor(alpha_soft, alpha_soft, alpha_tmp, ALU.add).then_inc(alpha_softplus, 1)
                dve.wait_ge(alpha_softplus, b + 1)
                V.tensor_scalar(log_alpha, alpha_soft, -1.0, None, ALU.mult).then_inc(log_alpha_ready, 1)
                for n in range(4):
                    k = 4 * b + n
                    nn = slice(n * 128, n * 128 + 128)
                    dve.wait_ge(chunk_keys, k + 1)
                    dve.wait_ge(tail_decays, b + 1)
                    if due(k):
                        dve.wait_ge(state_update, k)
                    V.tensor_tensor(k_decayed.rearrange('p (h d) -> p h d', d=64), flat(psum[:, 6:8, :]).rearrange('p (h d) -> p h d', d=64), tail_decay[:, n, :].unsqueeze(2).broadcast_to([PARTS, 16, 64]), ALU.mult).then_inc(chunk_keys_decayed, 1)
                    dve.wait_ge(head_decays, k + 1)
                    if due(k):
                        dve.wait_ge(chunk_out, k)
                    V.tensor_tensor(q_decayed, q_act[:, :, nn], head_decay, ALU.mult).then_inc(queries_decayed, 1)
                    dve.wait_ge(chunk_scores, k + 1)
                    dve.wait_ge(segment_decays, k + 1)
                    for q in range(2):
                        m = V.tensor_tensor(pair_scores[:, 8 * q:8 * q + 8, :], psum[:, 2 * q:2 * q + 2, :].rearrange('p a (b c) -> p (a b) c', c=128), pair_decay.rearrange('p (c q) k -> p q c k', q=2)[:, q], ALU.mult)
                    m.then_inc(chunk_scores_decayed, 1)
                    dve.wait_ge(chunk_out, k + 1)
                    dve.wait_ge(state_zeroed, b + 1)
                    if n > 0:
                        if due(k):
                            dve.wait_ge(state_ready, k)
                    V.tensor_tensor(state, state, head_decay[:, :, 127:128].broadcast_to([PARTS, 8, 64]), ALU.mult).then_inc(state_decayed, 1)
                    dve.wait_ge(state_update, k + 1)
                    dve.wait_ge(state_decayed, k + 1)
                    V.tensor_tensor(state, state, psum[:, 4, :].rearrange('p (c d) -> p c d', d=64), ALU.add).then_inc(state_ready, 1)
                dve.wait_ge(chunk_out_copied, 4 * b + 4)
                for c in range(8):
                    m = V.bn_stats(chan_stats[:, c, :], attn_heads[:, c, :])
                m.then_inc(norm_stats, 1)
                dve.wait_ge(norm_stats, b + 1)
                V.tensor_copy(group_tmp[:, 48:56], chan_stats[:, :, 1])
                for c in range(8):
                    m = V.bn_aggr(chan_mean_var[:, c, :], chan_stats[:, c, :])
                m.then_inc(norm_aggregated, 1)
                dve.wait_ge(group_means, b + 1)
                dve.wait_ge(norm_aggregated, b + 1)
                V.tensor_tensor(group_tmp[:, 0:8], chan_mean_var[:, :, 0], psum[:, 0, 0:8], ALU.subtract).then_inc(mean_offsets, 1)
                V.tensor_copy(group_tmp[:, 16:24], psum[:, 0, 0:8])
                dve.wait_ge(mean_offsets, b + 1)
                V.tensor_tensor(group_tmp[:, 8:16], group_tmp[:, 0:8], group_tmp[:, 0:8], ALU.mult).then_inc(mean_offsets_squared, 1)
                dve.wait_ge(mean_offsets_squared, b + 1)
                V.tensor_tensor(group_vars[:, 0, :], group_tmp[:, 8:16], chan_mean_var[:, :, 1], ALU.add).then_inc(group_spread, 1)
                dve.wait_ge(group_inverse, b + 1)
                V.tensor_tensor(group_tmp[:, 24:32], group_vars[:, 1, :], norm_affine[:, 0, :], ALU.mult).then_inc(group_scale, 1)
                dve.wait_ge(group_scale, b + 1)
                V.tensor_tensor(group_tmp[:, 32:40], group_tmp[:, 24:32], group_tmp[:, 16:24], ALU.mult).then_inc(group_shift, 1)
                dve.wait_ge(group_shift, b + 1)
                V.tensor_tensor(group_tmp[:, 40:48], norm_affine[:, 1, :], group_tmp[:, 32:40], ALU.subtract).then_inc(group_bias, 1)
                dve.wait_ge(group_bias, b + 1)
                for c in range(8):
                    V.tensor_scalar(attn_heads[:, c, :], attn_heads[:, c, :], group_tmp[:, 24 + c:25 + c], group_tmp[:, 40 + c:41 + c], ALU.mult, ALU.add).then_inc(heads_normed, 1)
                    dve.wait_ge(heads_normed, 8 * b + c + 1)
                    V.tensor_tensor(attn_heads[:, c, :], attn_heads[:, c, :], gate_act[:, c, :], ALU.mult).then_inc(heads_gated, 1)
                dve.wait_ge(attn_out, b + 1)
                V.tensor_tensor(normed[:, :], x_batch[:, :], psum[:, 2, :], ALU.add).then_inc(ln_input, 1)
                ln(2 * b, x_batch[:, :])
                dve.wait_ge(cross_logits, b + 1)
                V.tensor_reduce(cross_stat, psum[:, 3, 0:128].rearrange('p (a b) -> p a b', b=32), AX, ALU.max).then_inc(cross_max, 1)
                dve.wait_ge(cross_max, b + 1)
                V.tensor_tensor(cross_p, psum[:, 3, 0:128].rearrange('p (a b) -> p a b', b=32), cross_stat.unsqueeze(2).broadcast_to([PARTS, 4, 32]), ALU.subtract).then_inc(cross_shifted, 1)
                dve.wait_ge(cross_exp, b + 1)
                V.tensor_reduce(cross_stat, cross_p, AX, ALU.add).then_inc(cross_sum, 1)
                dve.wait_ge(cross_sum, b + 1)
                V.reciprocal(cross_stat, cross_stat).then_inc(cross_inverse, 1)
                dve.wait_ge(cross_inverse, b + 1)
                V.tensor_tensor(cross_p, cross_p, cross_stat.unsqueeze(2).broadcast_to([PARTS, 4, 32]), ALU.mult).then_inc(cross_probs, 1)
                V.tensor_copy(ctx_v_batch[0:32, :], ctx_v[0:32, bass.ds(b, 1), :].rearrange('p a b -> p (a b)')).then_inc(ctx_values_batch, 1)
                dve.wait_ge(cross_turned, b + 1)
                V.tensor_copy(cross_p_t[0:32, :], psum[0:32, 4, :]).then_inc(cross_turned_copied, 1)
                dve.wait_ge(cross_out, b + 1)
                V.tensor_tensor(normed[:, :], x_batch[:, :], psum[:, 5, :], ALU.add).then_inc(ln_input, 1)
                ln(2 * b + 1, x_all[:, bass.ds(b * 512, 512)])
                dve.wait_ge(ln_done, 2 * b + 2)
                V.tensor_copy(x_residual[:, bass.ds(b * 512, 512)], x_all[:, bass.ds(b * 512, 512)]).then_inc(x_updated, 1)

            def cross_setup():
                dve.wait_ge(ctx_keys, 1)
                V.tensor_scalar(ctx_k, psum[:, 0, 0:128], b_cross[:, 1:2], None, ALU.add).then_inc(ctx_keys_copied, 1)
                dve.wait_ge(ctx_folded, 1)
                V.tensor_copy(ctx_k_folded, psum[:, 1, 0:128]).then_inc(ctx_copied, 1)
                dve.wait_ge(ctx_bias, 1)
                V.tensor_copy(ctx_k_bias[0:1, :], psum[0:1, 2, 0:128]).then_inc(ctx_copied, 1)
                dve.wait_ge(ctx_values, 1)
                V.tensor_copy(ctx_v[0:32, :, :], psum[0:32, 3, :].rearrange('p (a b) -> p a b', b=128)).then_inc(ctx_copied, 1)
            dve.wait_ge(constants_loaded, 16 * 9)
            dve.wait_ge(x_loaded, 16)
            dve.wait_ge(attn_small_loaded, 16 * 9)
            V.tensor_copy(ident_bf16[:, :], ident[:, :]).then_inc(causal_bf16, 1)
            V.tensor_scalar(causal_bf16_mask[:, :], triangles[:, 0, :], -1.0, 1e+30, ALU.add, ALU.mult).then_inc(causal_bf16, 1)
            cross_setup()
            dve.wait_ge(ctx_copied, 3)
            ab(0)
            with dve.Fori(1, BATCHES) as b:
                ab(b)
            for g in range(4):
                step(g, g, None, True, g >= 1, g >= 2)
            for n in range(4):
                step(4 + n, n, 0, True, True, True)
            if FFN_PASSES > 2:
                with dve.Fori(1, FFN_PASSES - 1) as it:
                    for n in range(4):
                        step(it * 4 + (4 + n), n, it, True, True, True)
            for n in range(4):
                step(ALL_BLOCKS + n, n, FFN_PASSES - 1, False, n < 1, n < 2)
            for b in range(4):
                o = 8 + b
                if due(o):
                    dve.wait_ge(ln_done, o)
                dve.wait_ge(x_updated, FFN_PASSES + 4)
                V.tensor_tensor(normed[:, :], x_all[:, b * 512:b * 512 + 512], x_residual[:, b * 512:b * 512 + 512], ALU.add).then_inc(ln_input, 1)
                ln(o, x_all[:, b * 512:b * 512 + 512])

        @block.gpsimd
        def _(pool):
            U = nc.gpsimd
            for j, (ap, v) in enumerate(((x_shift[:, 0:32], 0.0), (x_shift[64:128, 32:33], 0.0), (ffn_x[64:128, 0:1], 0.0), (tiny[:, 0:1], 1e-05), (k_t[:, :, 0:32], 0.0))):
                if due(j):
                    pool.wait_ge(zeroed, j)
                U.memset(ap, v).then_inc(zeroed, 1)

            def stage(g, n):
                bt = g // 4
                o = bt % 4 * 512
                if due(g - 3 + 1):
                    pool.wait_ge(values_23, g - 3 + 1)
                pool.wait_ge(x_updated, bt + 1)
                U.tensor_copy(x_shift[0:64, 32 + n * 128:160 + n * 128], x_all[0:64, bass.ds(o + n * 128, 128)]).then_inc(block_shifted, 1)
                k = 1 if n == 0 else 0
                pool.wait_ge(block_shifted, g * 2 + 1)
                U.tensor_copy(x_shift[64:128, 32 + n * 128 + k:160 + n * 128], x_all[64:128, bass.ds(o + n * 128 + k - 1, 128 - k)]).then_inc(block_shifted, 1)

            def step(g, n, it, a, b, c, st):
                if a:
                    pool.wait_ge(block_shifted, 2 * g + 2)
                    pool.wait_ge(q_cos, g + 1)
                    pool.wait_ge(q_sin, g + 1)
                    U.tensor_tensor(cos_part[:, 0, :], cos_part[:, 0, :], sin_part[:, 0, :], ALU.add).then_inc(q_rotated, 1)
                    pool.wait_ge(k_cos, g + 1)
                    pool.wait_ge(k_sin, g + 1)
                    U.tensor_tensor(cos_part[:, 1, :], cos_part[:, 1, :], sin_part[:, 1, :], ALU.add).then_inc(k_rotated, 1)
                elif b and FFN_PASSES > 1:
                    pool.wait_ge(block_shifted, 2 * g + 2)
                if b:
                    if due(g):
                        pool.wait_ge(probs_inverse, g)
                    e3 = probs[:, :, :, :].rearrange('p c q k -> p (c q) k')
                    U.tensor_tensor(e3, e3, row_inv[:, :].unsqueeze(2).broadcast_to([PARTS, 16, 64]), ALU.mult).then_inc(probs_ready, 1)
                if st:
                    pool.wait_ge(k_rotated, g + 1)
                    if due(g):
                        pool.wait_ge(probs_ready, g)
                    stage(g + 1, (n + 1) % 4)
            pool.wait_ge(x_loaded, 16)
            pool.wait_ge(zeroed, 5)
            pool.wait_ge(attn_small_loaded, 16 * 9)

            def ab(b):
                for n in range(4):
                    k = 4 * b + n
                    pool.wait_ge(log_alpha_ready, b + 1)
                    if due(k):
                        pool.wait_ge(segment_sums, k)
                    U.tensor_tensor(seg_operand, triangles[:, 0, :].unsqueeze(1).broadcast_to([PARTS, 16, 128]), log_alpha[:, n * 16:n * 16 + 16].unsqueeze(2).broadcast_to([PARTS, 16, 128]), ALU.mult).then_inc(segment_operand, 1)
            ab(0)
            with pool.Fori(1, BATCHES) as b:
                ab(b)
            stage(0, 0)
            for g in range(4):
                step(g, g, None, True, g >= 1, g >= 2, FFN_PASSES > 1 or g < 3)
            for n in range(4):
                step(4 + n, n, 0, True, True, True, True)
            if FFN_PASSES > 2:
                with pool.Fori(1, FFN_PASSES - 1) as it:
                    for n in range(4):
                        step(it * 4 + (4 + n), n, it, True, True, True, True)
            for n in range(4):
                step(ALL_BLOCKS + n, n, FFN_PASSES - 1, False, n < 1, n < 2, False)

def shape_constants():
    n, dh = (512, 64)
    half = np.arange(0, dh, 2, dtype=np.float32)
    inv = (np.float32(1.0) / np.float32(10000.0) ** (half / np.float32(dh))).astype(np.float32)
    t = np.arange(n, dtype=np.float32)
    fr = t[:, None] * inv[None, :]
    fr = np.concatenate([fr, fr], -1)
    bs = (half + np.float32(0.4 * dh)) / np.float32(1.4 * dh)
    pw = (t - n // 2) / np.float32(16)
    sc = (bs[None, :] ** pw[:, None]).astype(np.float32)
    sc = np.concatenate([sc, sc], -1)
    sg = np.where(np.arange(64) < 32, -1, 1).astype(np.float32)
    cos, sin = (np.cos(fr), np.sin(fr))
    tb = np.stack([8 * cos * sc, 8 * sin * sc * sg, cos / sc, sin / sc * sg]).astype(np.float32)
    rotary_base = tb.reshape(4, 4, 128, 64).transpose(2, 0, 1, 3).copy()
    q = np.arange(128) % 32
    k = np.arange(64)
    ok = (k[None, :] >= q[:, None]) & (k[None, :] <= q[:, None] + 32)
    m1 = np.where(ok, 0, -1e+30).astype(np.float32)
    m0 = m1.copy()
    m0[0:32, 0:32] = -1e+30
    a = np.arange(128)
    tri = np.stack([a[:, None] <= a[None, :], a[:, None] > a[None, :]], 1).astype(np.float32)
    bd = (a[:, None] // 64 == a[None, :] // 64).astype(np.float32) / 64
    return dict(base=rotary_base, mask=np.stack([m0, m1], 1).copy(), ident=np.eye(128, dtype=np.float32), mean_w=np.full((128, 128), 1 / 128, np.float32), tri=tri, bd=bd, ones=np.ones((128, 128), np.float32))

def layout(a, LAYERS=6):
    layer_vecs = np.zeros((128, LAYERS, 9), np.float32)
    for l in range(LAYERS):
        for k, M in enumerate((128, 128, 85)):
            layer_vecs[:M, l, k] = a['L0_ffn_b1'][l, k * 128:k * 128 + M]
            layer_vecs[:M, l, 3 + k] = a['L0_ffn_b1'][l, 341 + k * 128:341 + k * 128 + M]
        layer_vecs[:, l, 6] = a['L0_ffn_ln_g'][l]
        layer_vecs[:, l, 7] = a['L0_ffn_ln_b'][l]
        layer_vecs[:, l, 8] = a['L0_ffn_b2'][l]
    sw = lambda v: np.concatenate([v[:, 32:], v[:, :32]], 1).copy()
    c = np.ascontiguousarray
    return dict(shape_constants(), x=c(a['x'].reshape(2048, 128).T), vec=layer_vecs.reshape(128, -1), qs=a['L0_ffn_q_scale'], qs_sw=sw(a['L0_ffn_q_scale']), ks=a['L0_ffn_k_scale'], ks_sw=sw(a['L0_ffn_k_scale']), wqkv=a['L0_ffn_Wqkv'], wo=a['L0_ffn_Wo'], w1=a['L0_ffn_W1'], w2=a['L0_ffn_W2'], a_wq=a['L0_attn_Wq'], a_wk=a['L0_attn_Wk'], a_wv=a['L0_attn_Wv'], a_wg=a['L0_attn_Wg'], a_wo=a['L0_attn_Wo'], a_wa=a['L0_attn_Wa'], a_ba=a['L0_attn_ba'].reshape(1, 16), a_gn=c(np.stack([a['L0_attn_gn_w'], a['L0_attn_gn_b']]).reshape(2, 8, 128).transpose(2, 0, 1)), ctx=c(a['ctx_1024'].reshape(128, 128).T), x_w=c(np.stack([a['L0_xattn_W2'].T, a['L0_xattn_W1'], a['L0_xattn_W3'].T], 1)), x_b=c(np.stack([a['L0_xattn_b1'], a['L0_xattn_b2']], 1)))


def kernel(**inputs):
    import numpy as _np
    import concourse.bacc as _bacc
    from concourse import mybir as _mybir
    from concourse.bass_utils import run_bass_kernel_spmd as _run

    nc = _bacc.Bacc("TRN2", target_bir_lowering=False, num_devices=1)
    arrays = {f"in_{name}": _np.ascontiguousarray(a) for name, a in layout({k: _np.asarray(v) for k, v in inputs.items()}).items()}
    io = {name[3:]: nc.dram_tensor(name, a.shape, _mybir.dt.from_np(a.dtype), kind="ExternalInput").ap()
          for name, a in arrays.items()}
    io["out"] = nc.dram_tensor("out_0_dram", (128, 2048), _mybir.dt.from_np(_np.dtype("float32")), kind="ExternalOutput").ap()
    decoder(nc, io)
    r = _run(nc, [arrays], core_ids=[0])
    got = r.results[0]["out_0_dram"]
    return _np.ascontiguousarray(got.T).reshape(4, 512, 128)
```
